# Optimizing a Trainium2 kernel written in Bass

```python
import numpy as np
import jax
import jax.numpy as jnp

def _softmax(x, axis=-1):
    return jax.nn.softmax(x, axis=axis)

def _gelu(x):
    return jax.nn.gelu(x, approximate=True)

def _silu(x):
    return jax.nn.silu(x)

def _sigmoid(x):
    return jax.nn.sigmoid(x)

def _layernorm(x, axis=-1, eps=1e-05):
    m = jnp.mean(x, axis=axis, keepdims=True)
    v = jnp.var(x, axis=axis, keepdims=True)
    return (x - m) / jnp.sqrt(v + eps)

def _scatter_add(tgt, idx, src, axis=0):
    return tgt.at[idx].add(src)

def _segment_sum(src, seg, n):
    return jax.ops.segment_sum(src, seg, n)
kernel_name = 'mk_xattn_ffn_d1_seqx_r4_ffe084'

def setup_inputs(seed: int=0):
    np.random.seed(seed)
    _w = jnp.asarray

    def _rec_inputs():
        import jax
        import jax.numpy as jnp
        _rk = jax.random.key(seed)
        x = -0.000125 + 0.9999 * jax.random.normal(jax.random.fold_in(_rk, 1), (16, 128, 1024), jnp.float32)
        _lenS = 128 - jax.random.randint(jax.random.fold_in(_rk, 7), (16,), 0, max(1, 128 // 4) + 1, jnp.int32)
        _lenS2 = 128 - jax.random.randint(jax.random.fold_in(_rk, 8), (16,), 0, max(1, 128 // 4) + 1, jnp.int32)
        _ctx_4096P = jax.random.normal(jax.random.fold_in(_rk, 11), (16, 16, 1024), jnp.float32)
        _ctx_4096c = jax.random.dirichlet(jax.random.fold_in(_rk, 511), 0.3 * jnp.ones((16,), jnp.float32), (16, 128))
        _ctx_4096t = jnp.einsum('bsk,bkd->bsd', _ctx_4096c, _ctx_4096P)
        _ctx_4096t = _ctx_4096t * jax.lax.rsqrt(jnp.mean(jnp.square(_ctx_4096t)) + 1e-12) * 0.953939
        ctx_4096 = -1.52775e-05 + 0.999936 * (_ctx_4096t + 0.3 * jax.random.normal(jax.random.fold_in(_rk, 611), (16, 128, 1024), jnp.float32))
        return (x, ctx_4096)
    x, ctx_4096 = _rec_inputs()

    def _L0_xattn_setup():
        import jax, jax.numpy as jnp
        import numpy as np
        H = 8
        C = 2

        def _autocorrelation(Q, K, V):
            B, L, D = Q.shape
            d = D // H
            q = Q.reshape(B, L, H, d).transpose(0, 2, 1, 3)
            k = K.reshape(B, L, H, d).transpose(0, 2, 1, 3)
            v = V.reshape(B, L, H, d).transpose(0, 2, 1, 3)
            qf = jnp.fft.fft(q, axis=2)
            kf = jnp.fft.fft(k, axis=2)
            corr = jnp.fft.ifft(qf * jnp.conj(kf), axis=2).real
            topk = int(C * np.log(L))
            w, idx = jax.lax.top_k(corr.transpose(0, 1, 3, 2), topk)
            w = jax.nn.softmax(w, axis=-1)
            pos = jnp.arange(L)[:, None]
            out = jnp.zeros_like(v)
            for i in range(topk):
                g = jnp.minimum(idx[:, :, None, :, i] + pos, L - 1)
                out = out + w[:, :, None, :, i] * jnp.take_along_axis(v, g, axis=2)
            return out.transpose(0, 2, 1, 3).reshape(B, L, D)
        key = jax.random.key(seed)
        k1, k2, k3 = jax.random.split(key, 3)
        B, L, D = (16, 128, 1024)
        Q = jax.random.normal(k1, (B, L, D), dtype=jnp.float32)
        K = jax.random.normal(k2, (B, L, D), dtype=jnp.float32)
        V = jax.random.normal(k3, (B, L, D), dtype=jnp.float32)
        return {'Q': Q, 'K': K, 'V': V}
    _L0_xattn_all = _L0_xattn_setup()
    _L0_xattn_in = {k: v for k, v in _L0_xattn_all.items() if k in ()}
    del _L0_xattn_all

    def _L0_ffn_setup():
        import jax, jax.numpy as jnp
        import numpy as np
        ALPHA = 32
        R = 16
        SCALING = ALPHA / R
        key = jax.random.key(seed)
        k1, k2, k3, k4 = jax.random.split(key, 4)
        B_, S, D = (4, 512, 1024)
        H, r, O = (8, R, 1024)
        x = jax.random.normal(k1, (B_, S, D), dtype=jnp.float32)
        A = jax.random.normal(k2, (H, r, D), dtype=jnp.float32) * 0.02
        Bm = jax.random.normal(k3, (H, O, r), dtype=jnp.float32) * 0.02
        Wr = jax.random.normal(k4, (H, D), dtype=jnp.float32) * 0.02
        br = jnp.zeros((H,), dtype=jnp.float32)
        return {'x': x, 'A': A, 'B': Bm, 'Wr': Wr, 'br': br}
    _L0_ffn_all = _L0_ffn_setup()
    _L0_ffn_in = {k: v for k, v in _L0_ffn_all.items() if k in ('A', 'B', 'Wr', 'br')}
    del _L0_ffn_all
    return {'x': x, 'ctx_4096': ctx_4096, 'L0_ffn_A': _L0_ffn_in['A'], 'L0_ffn_B': _L0_ffn_in['B'], 'L0_ffn_Wr': _L0_ffn_in['Wr'], 'L0_ffn_br': _L0_ffn_in['br']}

def reference(x, ctx_4096, L0_ffn_A, L0_ffn_B, L0_ffn_Wr, L0_ffn_br):
    import jax
    import jax.numpy as jnp

    def _L0_xattn_ref(Q, K, V):
        import jax, jax.numpy as jnp
        import numpy as np
        H = 8
        C = 2

        def _autocorrelation(Q, K, V):
            B, L, D = Q.shape
            d = D // H
            q = Q.reshape(B, L, H, d).transpose(0, 2, 1, 3)
            k = K.reshape(B, L, H, d).transpose(0, 2, 1, 3)
            v = V.reshape(B, L, H, d).transpose(0, 2, 1, 3)
            qf = jnp.fft.fft(q, axis=2)
            kf = jnp.fft.fft(k, axis=2)
            corr = jnp.fft.ifft(qf * jnp.conj(kf), axis=2).real
            topk = int(C * np.log(L))
            w, idx = jax.lax.top_k(corr.transpose(0, 1, 3, 2), topk)
            w = jax.nn.softmax(w, axis=-1)
            pos = jnp.arange(L)[:, None]
            out = jnp.zeros_like(v)
            for i in range(topk):
                g = jnp.minimum(idx[:, :, None, :, i] + pos, L - 1)
                out = out + w[:, :, None, :, i] * jnp.take_along_axis(v, g, axis=2)
            return out.transpose(0, 2, 1, 3).reshape(B, L, D)
        return _autocorrelation(Q, K, V)

    def _L0_ffn_ref(x, A, B, Wr, br):
        import jax, jax.numpy as jnp
        import numpy as np
        ALPHA = 32
        R = 16
        SCALING = ALPHA / R
        H = A.shape[0]
        router_logits = jnp.einsum('bsd,hd->bsh', x, Wr) + br
        scores = H * jax.nn.softmax(router_logits, axis=-1)
        low = jnp.einsum('bsd,hrd->bshr', x, A)
        out = jnp.einsum('bshr,hor,bsh->bso', low, B, scores)
        return SCALING * out
    x = x + _L0_xattn_ref(_layernorm(x, axis=-1), ctx_4096, ctx_4096)
    x = x + _L0_ffn_ref(_layernorm(x, axis=-1), L0_ffn_A, L0_ffn_B, L0_ffn_Wr, L0_ffn_br)
    return x

_drawn_inputs = setup_inputs


def setup_inputs(seed=0):
    import zlib

    import numpy as np

    out = dict(_drawn_inputs(seed))
    spreads = {'L0_ffn_br': (0.0, 0.1)}
    factors = {}
    for name, (base, spread) in spreads.items():
        noise = np.random.default_rng([zlib.crc32(name.encode()), seed]).standard_normal(out[name].shape)
        drawn = base * np.exp(spread * noise) if base else spread * noise
        out[name] = jnp.asarray(drawn.astype(out[name].dtype))
    for name, factor in factors.items():
        out[name] = (out[name] * factor).astype(out[name].dtype)
    return out
```

```python
from contextlib import ExitStack

import numpy as np
import concourse.bass as bass
from concourse import mybir
from concourse.alu_op_type import AluOpType as ALU

FP32 = mybir.dt.float32
FP32R = mybir.dt.float32r
ACT = mybir.ActivationFunctionType
AX = mybir.AxisListType

NSEQ, L, D = 16, 128, 1024
GW = 512
NT = GW // 128
NG = NSEQ * D // GW
HEADS, RANK = 8, 16
HR = HEADS * RANK
LOWN = HR + HEADS
DC = D // 128
GAIN = float(HEADS) * 32.0 / RANK
TOPK = int(2 * np.log(L))
EPS = 1e-5
NEG = -3.0e38
SLOTS = 4
FIRST = 7
LOOPS = 5
SETS = ["F", "G", "Gv", "C1", "C2", "D1", "D2", "D3", "D4", "I"]


def dft_matrices():
    n = np.arange(L)
    even = np.outer(np.arange(1, 64), n) * (2 * np.pi / L)
    odd = np.outer(2 * np.arange(64) + 1, n) * (np.pi / L)
    alt = (-1.0) ** n
    F = np.concatenate([np.ones((1, L)), np.cos(even), alt[None], -np.sin(even)])
    G = np.concatenate([np.cos(odd), -np.sin(odd)])
    Gv = G.copy()
    Gv[:, L - 1] -= G.sum(1)
    C1 = np.concatenate([np.ones((1, L)), 2 * np.cos(even), alt[None], 2 * np.cos(even)]) / L
    zero = np.zeros((1, L))
    C2 = np.concatenate([zero, 2 * np.sin(even), zero, -2 * np.sin(even)]) / L
    D1 = C1 / 2
    D2 = -C2 / 2
    D2[0] = 0.5
    D3 = np.concatenate([np.cos(odd), np.cos(odd)]) / L
    D4 = np.concatenate([-np.sin(odd), np.sin(odd)]) / L
    mats = dict(F=F.T, G=G.T, Gv=Gv.T, C1=C1, C2=C2, D1=D1, D2=D2, D3=D3, D4=D4, I=np.eye(L))
    return np.ascontiguousarray(np.concatenate([mats[k] for k in SETS], 1).astype(np.float32))


def build(nc, x, ctx, A, B, Wr, br, mats, out):
    es = ExitStack()
    with es:
        def sb(name, shape, dtype=FP32):
            return es.enter_context(nc.sbuf_tensor(name, shape, dtype))

        def ps(name, shape):
            return es.enter_context(nc.psum_tensor(name, shape, FP32))

        def sem(name):
            return es.enter_context(nc.semaphore(name))

        M_sb = sb("M_sb", [128, len(SETS) * L])
        M = {k: M_sb[:, i * L:(i + 1) * L] for i, k in enumerate(SETS)}
        SPLIT = ["F", "G", "Gv"]
        Mhl = [sb(f"M{p}", [128, len(SPLIT) * L], FP32R) for p in ("hi", "lo")]
        MS = {k: [m[:, i * L:(i + 1) * L] for m in Mhl] for i, k in enumerate(SPLIT)}
        X = sb("X", [128, NSEQ * D])
        CTX = [sb(f"CTX{i}", [128, D]) for i in range(2)]
        Chl = [[sb(f"C{p}{i}", [128, GW], FP32R) for p in ("hi", "lo")] for i in range(2)]
        q = [sb(f"q{i}", [128, GW]) for i in range(2)]
        K = [sb(f"K{i}", [128, GW]) for i in range(SLOTS)]
        Ks = [sb(f"Ks{i}", [128, GW]) for i in range(SLOTS)]
        V = [sb(f"V{i}", [128, GW]) for i in range(SLOTS)]
        Vs = [sb(f"Vs{i}", [128, GW]) for i in range(SLOTS)]
        QK = [sb(f"QK{i}", [128, 2, GW]) for i in range(2)]
        top8 = sb("top8", [128, NT, 8])
        ninth = sb("ninth", [128, NT, 8])
        left1 = sb("left1", [128, NT, L])
        left2 = [sb(f"left2{i}", [128, NT, L]) for i in range(2)]
        E = [sb(f"E{i}", [128, NT, L]) for i in range(2)]
        dtop = sb("dtop", [128, NT, TOPK])
        etop = sb("etop", [128, NT, TOPK])
        stop = sb("stop", [128, NT])
        lnsum = sb("lnsum", [128, NT])
        shift = [sb(f"shift{i}", [128, NT]) for i in range(2)]
        WT = [sb(f"WT{i}", [128, GW]) for i in range(2)]
        WThl = [[sb(f"WT{p}{i}", [128, GW], FP32R) for p in ("hi", "lo")] for i in range(2)]
        PW = [sb(f"PW{i}", [128, 4, GW]) for i in range(2)]
        x2 = [sb(f"x2{i}", [128, D]) for i in range(2)]
        xT = [sb(f"xT{i}", [128, GW]) for i in range(2)]
        ABT = sb("ABT", [128, DC, LOWN])
        BT = sb("BT", [128, D])
        BThl = [sb(f"BT{p}", [128, D], FP32R) for p in ("hi", "lo")]
        pw = [p[:, :, :].rearrange("p (a b) c -> p a (b c)", a=2) for p in PW]
        A_sb, W_sb = pw[0][:, 0, :], pw[0][0:HEADS, 1, :]
        B_sb = pw[1][:, 0, :].rearrange("p (h c r) -> p h c r", h=HEADS, r=RANK)
        B_by = pw[1][:, 1, :].rearrange("p (c h r) -> p c h r", h=HEADS, r=RANK)
        br_sb = sb("br_sb", [128, HEADS])
        amean = sb("amean", [128, 2])
        consts = sb("consts", [128, 3])
        ast = sb("ast", [128, 2, 6])
        st1 = sb("st1", [128, 2, 6])
        mv1 = [sb(f"mv1{i}", [128, 2]) for i in range(2)]
        nm1 = sb("nm1", [128, 2])
        rs1 = [sb(f"rs1{i}", [128, 2]) for i in range(2)]
        st2 = sb("st2", [128, 2, 6])
        mv2 = sb("mv2", [128, 2])
        ve2 = sb("ve2", [128, 1])
        rs2 = sb("rs2", [128, 1])
        lraw = sb("lraw", [128, HEADS])
        lg = sb("lg", [128, HEADS])
        lmax = sb("lmax", [128, 1])
        le = sb("le", [128, HEADS])
        lsum = sb("lsum", [128, 1])
        lrec = sb("lrec", [128, 1])
        sc = sb("sc", [128, HEADS])
        z = sb("z", [128, HEADS, RANK])
        ffn = sb("ffn", [128, D])
        zThl = [sb(f"zT{p}", [128, 128], FP32R) for p in ("hi", "lo")]

        pKV = ps("pKV", [128, GW])
        pQ = ps("pQ", [128, GW])
        pC = ps("pC", [128, NT, L])
        pT = ps("pT", [128, GW])
        pWc = ps("pWc", [128, GW])
        pWn = ps("pWn", [128, GW])
        pO = ps("pO", [128, GW])
        pL = ps("pL", [128, GW])
        setup_banks = (pT, pO, pWc, pWn)
        pLow, pZ = pL[:, 0:LOWN], pL[:, 256:384]

        d_mat, d_AW, d_B = sem("d_mat"), sem("d_AW"), sem("d_B")
        d_x = [sem(f"d_x{i}") for i in range(2)]
        d_ctx = [sem(f"d_ctx{i}") for i in range(2)]
        d_ks = [sem(f"d_ks{i}") for i in range(SLOTS)]
        d_vs = [sem(f"d_vs{i}") for i in range(SLOTS)]
        d_out = sem("d_out")
        t_setup, t_K, t_Q, t_V, t_C, t_WT, t_Wc, t_Wn, t_O, t_XT, t_low, t_zT, t_F = (
            sem("t_" + n) for n in "setup K Q V C WT Wc Wn O XT low zT F".split())
        a_setup, a_q, a_K, a_V, a_etop, a_ln, a_E, a_left, a_F, a_WT, a_WThi, a_Chi, a_XT, a_le, a_zT = (
            sem("a_" + n) for n in "setup q K V etop ln E left F WT WThi Chi XT le zT".split())
        v_setup, v_stat, v_stats, v_QK, v_top, v_left1, v_nine, v_left2, v_dtop, v_stop, v_shift0, v_shift = (
            sem("v_" + n) for n in "setup stat stats QK top left1 nine left2 dtop stop shift0 shift".split())
        v_PW, v_x2, v_st, v_mv2, v_lraw, v_lmax, v_lg, v_lrec, v_sc, v_z, v_zTlo, v_BT, v_M, v_prep, v_init, v_apart = (
            sem("v_" + n) for n in "PW x2 st mv2 lraw lmax lg lrec sc z zTlo BT M prep init apart".split())
        g_B, g_WTlo, g_out, g_setup, g_rsa, g_rs1, g_W, g_rsb, g_rs2 = (sem("g_" + n) for n in "B WTlo out setup rsa rs1 W rsb rs2".split())

        c_Clo = sem("c_Clo")

        block = es.enter_context(nc.Block())

        class At:

            def __init__(self, j, off):
                self.j, self.off = j, off
                self.half = off % 2
                self.r2, self.r4 = off % 2, off % 4
                self.seq_r2 = off // 2 % 2

            def __sub__(self, lag):
                return At(self.j, self.off - lag)

            def exists(self):
                return not isinstance(self.j, int) or 0 <= SLOTS * self.j + self.off < NG

            def count(self, each=1, more=0):
                return self.j * (SLOTS * each) + ((self.off + 1) * each + more)

            def seqs(self, each=1, more=0):
                return self.j * (SLOTS // 2 * each) + ((self.off // 2 + 1) * each + more)

            def turns(self, each):
                return self.j * each + (self.off // SLOTS + 1) * each

            def seq(self):
                return self.j * (SLOTS // 2) + self.off // 2

            def col(self, half=0):
                return self.j * (SLOTS // 2 * D) + (self.off // 2 * D + half * GW)

        def wait(eng, semaphore, value):
            if not isinstance(value, int) or value > 0:
                eng.wait_ge(semaphore, value)

        def wait_apart(eng, semaphore, value):
            wait(eng, semaphore, value)
            if not isinstance(value, int):
                eng.sem_inc(v_apart, 1)

        def split_product(bank, left, right):
            (lh, ll), (rh, rl) = left, right
            nc.tensor.matmul(bank, lh, rh, start=True, stop=False)
            nc.tensor.matmul(bank, lh, rl, start=False, stop=False)
            return nc.tensor.matmul(bank, ll, rh, start=False, stop=True)

        def slots(eng, one_slot, setup={}):
            for s in range(-1, FIRST):
                if s in setup:
                    setup[s]()
                one_slot(At(0, s))
            with eng.Fori(0, LOOPS) as j:
                for k in range(SLOTS):
                    one_slot(At(j, FIRST + k))
            for s in range(FIRST, NG + 5 - SLOTS * LOOPS):
                one_slot(At(LOOPS, s))

        cols = [slice(h * GW, (h + 1) * GW) for h in range(2)]
        tiles = [slice(t * 128, (t + 1) * 128) for t in range(NT)]

        @block.sync
        def _(sp):
            sp.dma_start(X[:, 0:D], x[0]).then_inc(d_x[0], 16)
            sp.dma_start(M_sb[:, :], mats).then_inc(d_mat, 16)
            sp.dma_start(CTX[0][:, :], ctx[0]).then_inc(d_ctx[0], 16)
            sp.dma_start(A_sb, A.rearrange("h r d -> (h r) d")).then_inc(d_AW, 16)
            sp.dma_start(W_sb, Wr).then_inc(d_AW, 16)
            sp.dma_start(CTX[1][:, :], ctx[1]).then_inc(d_ctx[1], 16)
            sp.dma_start(br_sb[:, :], br.partition_broadcast(128)).then_inc(d_B, 16)
            sp.dma_start(B_sb.rearrange("p h c r -> p h (c r)"),
                         B.rearrange("h (p c) r -> p h (c r)", p=128)).then_inc(d_B, 16)
            sp.dma_start(X[:, D:2 * D], x[1]).then_inc(d_x[1], 16)
            sp.wait_ge(d_x[0], 16)
            sp.dma_start(X[:, 2 * D:3 * D], x[2]).then_inc(d_x[0], 16)

            def slot(s):
                nxt = s - (-6)
                if s.half == 1 and s.exists() and nxt.exists():
                    r = nxt.seq_r2
                    wait(sp, d_x[r], (s - (-2)).turns(16))
                    sp.dma_start(X[:, bass.ds(nxt.col(), D)],
                                 x[bass.ds(nxt.seq(), 1)].rearrange("a p d -> (a p) d")).then_inc(d_x[r], 16)
                if s.exists():
                    r = s.r4
                    wait(sp, a_K, s.count())
                    sp.dma_start(Ks[r][1:64, :], K[r][65:128, :]).then_inc(d_ks[r], 16)
                    sp.dma_start(Ks[r][64:128, :], K[r][0:64, :]).then_inc(d_ks[r], 16)
                    sp.dma_start(Ks[r][0:1, :], CTX[s.seq_r2][127:128, cols[s.half]]).then_inc(d_ks[r], 16)
                    wait(sp, a_V, s.count())
                    sp.dma_start(Vs[r][0:64, :], V[r][64:128, :]).then_inc(d_vs[r], 16)
                    sp.dma_start(Vs[r][64:128, :], V[r][0:64, :]).then_inc(d_vs[r], 16)
                nxt = s - (-4)
                if s.half == 1 and s.exists() and nxt.exists():
                    r = s.seq_r2
                    for g in (s - 1, s):
                        wait(sp, d_ks[g.r4], g.turns(48))
                    sp.dma_start(CTX[r][:, :],
                                 ctx[bass.ds(nxt.seq(), 1)].rearrange("a p d -> (a p) d")).then_inc(d_ctx[r], 16)
                f = s - 5
                if f.half == 1 and f.exists():
                    wait(sp, g_out, f.seqs(2))
                    sp.dma_start(out[bass.ds(f.seq(), 1)].rearrange("a p d -> (a p) d"),
                                 X[:, bass.ds(f.col(), D)]).then_inc(d_out, 16)

            slots(sp, slot)
            sp.wait_ge(d_out, 16 * NSEQ)

        @block.tensor
        def _(pe):
            mm = nc.tensor.matmul

            def weights_A():
                pe.wait_ge(v_setup, 1)
                for u in range(DC // 2):
                    for c in (2 * u, 2 * u + 1):
                        at, to = slice(c * 128, (c + 1) * 128), c % 2 * LOWN
                        nc.tensor.transpose(setup_banks[u][:, to:to + HR], A_sb[:, at], M["I"])
                        last = nc.tensor.transpose(setup_banks[u][:, to + HR:to + LOWN], W_sb[:, at],
                                                   M["I"][0:HEADS, 0:HEADS])
                    last.then_inc(t_setup, 1)

            def weights_B():
                pe.wait_ge(g_B, 1)
                pe.wait_ge(a_setup, DC // 2)
                for u in range(2):
                    for c in range(4):
                        last = nc.tensor.transpose(setup_banks[2 + u][:, tiles[c]],
                                                   B_by[:, 4 * u + c, :, :].rearrange("p h r -> p (h r)"), M["I"])
                    last.then_inc(t_setup, 1)

            def slot(s):
                c, g, h, e, f = s - 1, s - 2, s - 3, s - 4, s - 5
                if e.exists():
                    wait(pe, v_x2, e.count())
                    for t in range(NT):
                        at = e.half * GW + t * 128
                        last = nc.tensor.transpose(pO[:, tiles[t]], x2[e.seq_r2][:, at:at + 128], M["I"])
                    last.then_inc(t_XT, 1)
                if s.exists():
                    ctx_halves = [m[:, :] for m in Chl[s.r2]]
                    wait(pe, c_Clo, s.count())
                    wait(pe, a_V, s.count(1, -1))
                    split_product(pKV[:, :], MS["F"], ctx_halves).then_inc(t_K, 1)
                if c.exists():
                    wait(pe, v_QK, c.count(2))
                    wait(pe, a_E, c.count(2, -2))
                    for t in range(NT):
                        mm(pC[:, t, :], QK[c.r2][:, 0, tiles[t]], M["C1"], start=True, stop=False)
                        last = mm(pC[:, t, :], QK[c.r2][:, 1, tiles[t]], M["C2"], start=False, stop=True)
                    last.then_inc(t_C, 1)
                if g.exists():
                    wait(pe, g_W, g.count(2))
                    for t in range(NT):
                        last = nc.tensor.transpose(pT[:, tiles[t]], E[g.r2][:, t, :], M["I"])
                    last.then_inc(t_WT, 1)
                if e.exists():
                    wait(pe, a_XT, e.count())
                    if e.half == 0:
                        wait(pe, v_zTlo, e.seqs(1, -1))
                    for t in range(NT):
                        chunk = e.half * NT + t
                        last = mm(pLow, xT[e.r2][:, tiles[t]], ABT[:, chunk, :],
                                  start=(chunk == 0), stop=(chunk == DC - 1))
                    if e.half == 1:
                        last.then_inc(t_low, 1)
                if h.exists():
                    for p, name in enumerate(("D1", "D2", "D3", "D4")):
                        wait(pe, v_PW, h.count(4, p - 3))
                        last = mm(pO[:, :], M[name], PW[h.r2][:, p, :], start=(p == 0), stop=(p == 3))
                    last.then_inc(t_O, 1)
                if f.half == 1 and f.exists():
                    wait(pe, v_zTlo, f.seqs())
                    if h.exists():
                        wait(pe, v_PW, h.count(4))
                    for b, bank in enumerate((pWc, pWn)):
                        split_product(bank[:, :], [m[:, :] for m in zThl], [m[:, cols[b]] for m in BThl])\
                            .then_inc(t_F, 1)
                if s.exists():
                    wait(pe, a_q, s.count())
                    wait(pe, v_QK, s.count(2, -2))
                    mm(pQ[:, :], M["F"], q[s.r2][:, :], start=True, stop=True).then_inc(t_Q, 1)
                    wait(pe, a_K, s.count())
                    split_product(pKV[:, :], MS["Gv"], ctx_halves).then_inc(t_V, 1)
                if g.exists():
                    w_halves = [m[:, :] for m in WThl[g.r2]]
                    wait(pe, g_WTlo, g.count())
                    if not h.exists():
                        wait(pe, a_setup, DC // 2 + 2)
                    if f.half == 1 and f.exists():
                        wait(pe, a_F, f.seqs(2, -1))
                    split_product(pWc[:, :], MS["F"], w_halves).then_inc(t_Wc, 1)
                    if f.half == 1 and f.exists():
                        wait(pe, a_F, f.seqs(2))
                    split_product(pWn[:, :], MS["G"], w_halves).then_inc(t_Wn, 1)
                if e.half == 1 and e.exists():
                    wait(pe, v_z, e.seqs())
                    nc.tensor.transpose(pZ, z[:, :, :].rearrange("p h r -> p (h r)"), M["I"]).then_inc(t_zT, 1)

            pe.wait_ge(d_mat, 16)
            pe.wait_ge(v_M, 2)
            slots(pe, slot, {1: weights_A, 2: weights_B, 4: lambda: pe.wait_ge(v_BT, 2)})

        @block.scalar
        def _(act):
            act.preload_act_table_set("natural_log_exp_and_others")

            def weights_A():
                for u in range(DC // 2):
                    act.wait_ge(t_setup, u + 1)
                    act.copy(ABT[:, 2 * u:2 * u + 2, :],
                             setup_banks[u][:, 0:2 * LOWN].rearrange("p (c n) -> p c n", c=2)).then_inc(a_setup, 1)

            def weights_B():
                for u in range(2):
                    act.wait_ge(t_setup, DC // 2 + u + 1)
                    act.copy(BT[:, :].rearrange("k (p c) -> k c p", c=DC)[:, 4 * u:4 * u + 4, :],
                             setup_banks[2 + u][:, :].rearrange("k (c p) -> k c p", c=4)).then_inc(a_setup, 1)

            def leave(s):
                e, n = s - 4, s - (-1)
                if s.exists():
                    wait(act, t_V, s.count())
                    act.copy(V[s.r4][:, :], pKV[:, :]).then_inc(a_V, 1)
                if e.half == 1 and e.exists():
                    wait(act, t_zT, e.seqs())
                    act.copy(zThl[0][:, :], pZ).then_inc(a_zT, 1)
                if n.exists():
                    wait(act, g_rs1, n.seqs())
                    act.activation(q[n.r2][:, :], X[:, bass.ds(n.col(n.half), GW)], ACT.Identity,
                                   bias=rs1[n.seq_r2][:, 1:2], scale=rs1[n.seq_r2][:, 0:1]).then_inc(a_q, 1)

            def slot(s):
                c, g, e, f, n = s - 1, s - 2, s - 4, s - 5, s - (-1)
                if e.exists():
                    wait(act, t_XT, e.count())
                    act.copy(xT[e.r2][:, :], pO[:, :]).then_inc(a_XT, 1)
                if s.exists():
                    wait(act, t_K, s.count())
                    act.copy(K[s.r4][:, :], pKV[:, :]).then_inc(a_K, 1)
                if n.exists():
                    if n.half == 0:
                        wait(act, d_ctx[n.seq_r2], n.turns(16))
                    act.copy(Chl[n.r2][0][:, :], CTX[n.seq_r2][:, cols[n.half]]).then_inc(a_Chi, 1)
                if g.exists():
                    wait(act, t_WT, g.count())
                    act.copy(WThl[g.r2][0][:, :], pT[:, :]).then_inc(a_WThi, 1)
                    act.copy(WT[g.r2][:, :], pT[:, :]).then_inc(a_WT, 1)
                early = c.exists() and not g.exists()
                if early:
                    leave(s)
                if c.exists():
                    wait(act, v_dtop, c.count())
                    act.activation(etop[:, :, :], dtop[:, :, :], ACT.Exp).then_inc(a_etop, 1)
                if c.exists():
                    wait(act, v_stop, c.count())
                    act.activation(lnsum[:, :], stop[:, :], ACT.Ln).then_inc(a_ln, 1)
                for u in range(2):
                    if c.exists():
                        wait(act, v_shift, c.count())
                        for t in (2 * u, 2 * u + 1):
                            last = act.activation(E[c.r2][:, t, :], pC[:, t, :], ACT.Exp,
                                                  bias=shift[c.r2][:, t:t + 1])
                        last.then_inc(a_E, 1)
                        for t in (2 * u, 2 * u + 1):
                            last = act.activation(left2[c.r2][:, t, :], left2[c.r2][:, t, :], ACT.Exp,
                                                  bias=shift[c.r2][:, t:t + 1])
                        last.then_inc(a_left, 1)
                    if u == 0 and e.half == 1 and e.exists():
                        wait(act, v_lg, e.seqs())
                        act.activation(le[:, :], lg[:, :], ACT.Exp, accum_out=lsum[:, :]).then_inc(a_le, 1)
                    if f.half == 1 and f.exists():
                        wait(act, g_out, f.seqs(2, u - 3))
                        wait(act, t_F, f.seqs(2, u - 1))
                        act.copy(ffn[:, cols[u]], (pWc, pWn)[u][:, :]).then_inc(a_F, 1)
                if not early:
                    leave(s)

            slots(act, slot, {1: weights_A, 2: weights_B})

        @block.gpsimd
        def _(pool):
            def rstd(n):
                mv, rs = mv1[n.seq_r2], rs1[n.seq_r2]
                wait(pool, v_stats, n.seqs())
                pool.tensor_tensor(nm1[:, 0:1], mv[:, 0:1], consts[:, 1:2], ALU.mult).then_inc(g_rsa, 1)
                pool.tensor_tensor(nm1[:, 1:2], mv[:, 1:2], consts[:, 2:3], ALU.add).then_inc(g_rsa, 1)
                wait(pool, g_rsa, n.seqs(3, -1))
                pool.tensor_tensor(rs[:, 0:1], nm1[:, 1:2], consts[:, 0:1], ALU.pow).then_inc(g_rsa, 1)
                wait(pool, g_rsa, n.seqs(3))
                pool.tensor_tensor(rs[:, 1:2], nm1[:, 0:1], rs[:, 0:1], ALU.mult).then_inc(g_rs1, 1)

            def slot(s):
                c, g, h, f, n = s - 1, s - 2, s - 3, s - 5, s - (-1)
                if s.exists() and n.exists():
                    hi, lo = Chl[n.r2]
                    wait(pool, a_Chi, n.count())
                    pool.tensor_tensor(lo[:, :], CTX[n.seq_r2][:, cols[n.half]], hi[:, :].bitcast(FP32),
                                       ALU.subtract).then_inc(c_Clo, 1)
                if g.exists():
                    hi, lo = WThl[g.r2]
                    wait(pool, a_WT, g.count())
                    pool.tensor_tensor(lo[:, :], WT[g.r2][:, :], hi[:, :].bitcast(FP32),
                                       ALU.subtract).then_inc(g_WTlo, 1)
                if n.half == 0 and n.exists():
                    rstd(n)
                if c.exists():
                    for u in range(2):
                        at = slice(2 * u, 2 * u + 2)
                        wait(pool, a_left, c.count(2, u - 1))
                        pool.tensor_tensor(E[c.r2][:, at, :], E[c.r2][:, at, :], left2[c.r2][:, at, :],
                                           ALU.subtract).then_inc(g_W, 1)
                if h.half == 1 and h.exists():
                    wait(pool, v_mv2, h.seqs())
                    pool.tensor_tensor(ve2[:, :], mv2[:, 1:2], consts[:, 2:3], ALU.add).then_inc(g_rsb, 1)
                    wait(pool, g_rsb, h.seqs())
                    pool.tensor_tensor(rs2[:, :], ve2[:, :], consts[:, 0:1], ALU.pow).then_inc(g_rs2, 1)
                if f.half == 1 and f.exists():
                    for b in range(2):
                        wait(pool, a_F, f.seqs(2, b - 1))
                        pool.tensor_tensor(X[:, bass.ds(f.col(b), GW)], ffn[:, cols[b]],
                                           x2[f.seq_r2][:, cols[b]], ALU.add).then_inc(g_out, 1)

            for i, value in enumerate((-0.5, -1.0, EPS)):
                pool.memset(consts[:, i:i + 1], value).then_inc(g_setup, 1)
            pool.wait_ge(g_setup, 3)

            def weights():
                pool.wait_ge(d_B, 32)
                pool.tensor_copy(B_by.rearrange("p c h r -> p h c r"), B_sb).then_inc(g_B, 1)

            slots(pool, slot, {1: weights})

        @block.vector
        def _(dve):
            def weights():
                dve.wait_ge(d_AW, 32)
                done = 0
                for rows, m in ((HR, A_sb), (HEADS, W_sb)):
                    dve.bn_stats(ast[0:rows, 0, :], m[:, cols[0]]).then_inc(v_prep, 1)
                    dve.bn_stats(ast[0:rows, 1, :], m[:, cols[1]]).then_inc(v_prep, 1)
                    dve.wait_ge(v_prep, done + 2)
                    dve.bn_aggr(amean[0:rows, :], ast[0:rows, :, :]).then_inc(v_prep, 1)
                    dve.wait_ge(v_prep, done + 3)
                    dve.tensor_scalar(m[:, :], m[:, :], amean[0:rows, 0:1], None, ALU.subtract).then_inc(v_prep, 1)
                    done += 4
                    dve.wait_ge(v_prep, done)
                dve.memset(lmax[:, :], 0.0).then_inc(v_setup, 1)

            def first_slot():
                dve.wait_ge(d_mat, 16)
                n = len(SPLIT) * L
                dve.tensor_copy(Mhl[0][:, :], M_sb[:, 0:n]).then_inc(v_M, 1)
                dve.wait_ge(v_M, 1)
                dve.tensor_tensor(Mhl[1][:, :], M_sb[:, 0:n], Mhl[0][:, :].bitcast(FP32), ALU.subtract)\
                    .then_inc(v_M, 1)
                hi, lo = Chl[0]
                dve.wait_ge(a_Chi, 1)
                dve.tensor_tensor(lo[:, :], CTX[0][:, cols[0]], hi[:, :].bitcast(FP32), ALU.subtract).then_inc(c_Clo, 1)
                weights()

            def split_B():
                dve.wait_ge(a_setup, DC // 2 + 2)
                dve.tensor_copy(BThl[0][:, :], BT[:, :]).then_inc(v_BT, 1)
                dve.wait_ge(v_BT, 1)
                dve.tensor_tensor(BThl[1][:, :], BT[:, :], BThl[0][:, :].bitcast(FP32), ALU.subtract).then_inc(v_BT, 1)

            def statistics(n):
                wait(dve, d_x[n.seq_r2], n.turns(16))
                for b in range(2):
                    dve.bn_stats(st1[:, b, :], X[:, bass.ds(n.col(b), GW)]).then_inc(v_stat, 1)
                wait_apart(dve, v_stat, n.seqs(2))
                dve.bn_aggr(mv1[n.seq_r2][:, :], st1[:, :, :]).then_inc(v_stats, 1)

            def products(s):
                wait(dve, t_Q, s.count())
                wait(dve, a_K, s.count())
                dve.tensor_tensor(QK[s.r2][:, 0, :], pQ[:, :], K[s.r4][:, :], ALU.mult).then_inc(v_QK, 1)
                wait(dve, d_ks[s.r4], s.turns(48))
                dve.tensor_tensor(QK[s.r2][:, 1, :], pQ[:, :], Ks[s.r4][:, :], ALU.mult).then_inc(v_QK, 1)

            def slot(s):
                c, h, e, nxt = s - 1, s - 3, s - 4, s - (-2)
                ffn_here = e.half == 1 and e.exists()
                if h.exists():
                    r = h.r4
                    wait(dve, t_Wc, h.count())
                    dve.tensor_tensor(PW[h.r2][:, 0, :], pWc[:, :], K[r][:, :], ALU.mult).then_inc(v_PW, 1)
                    dve.tensor_tensor(PW[h.r2][:, 1, :], pWc[:, :], Ks[r][:, :], ALU.mult).then_inc(v_PW, 1)
                    wait(dve, t_Wn, h.count())
                    wait(dve, a_V, h.count())
                    dve.tensor_tensor(PW[h.r2][:, 2, :], pWn[:, :], V[r][:, :], ALU.mult).then_inc(v_PW, 1)
                    wait(dve, d_vs[r], h.turns(32))
                    dve.tensor_tensor(PW[h.r2][:, 3, :], pWn[:, :], Vs[r][:, :], ALU.mult).then_inc(v_PW, 1)
                early = c.exists() and not (s - 2).exists()
                if early:
                    products(s)
                if c.exists():
                    wait_apart(dve, t_C, c.count())
                    for t in range(NT):
                        dve.max(top8[:, t, :], pC[:, t, :]).then_inc(v_top, 1)
                    wait_apart(dve, v_top, c.count(NT))
                    for t in range(NT):
                        dve.match_replace(left1[:, t, :], top8[:, t, :], pC[:, t, :], NEG).then_inc(v_left1, 1)
                    wait(dve, v_left1, c.count(NT))
                    dve.reduce_max(ninth[:, :, 0:1], left1[:, :, :], AX.X).then_inc(v_nine, 1)
                    wait_apart(dve, v_nine, c.count())
                    dve.tensor_tensor(dtop[:, :, 0:8], top8[:, :, :], top8[:, :, 0:1].broadcast_to([128, NT, 8]),
                                      ALU.subtract)
                    dve.tensor_tensor(dtop[:, :, 8:9], ninth[:, :, 0:1], top8[:, :, 0:1],
                                      ALU.subtract).then_inc(v_dtop, 1)
                    for t in range(NT):
                        dve.match_replace(left2[c.r2][:, t, :], ninth[:, t, :], left1[:, t, :], NEG)\
                           .then_inc(v_left2, 1)
                    wait(dve, a_etop, c.count())
                    dve.reduce_sum(stop[:, :], etop[:, :, :], AX.X).then_inc(v_stop, 1)
                if ffn_here:
                    wait(dve, t_low, e.seqs())
                    wait(dve, g_rs2, e.seqs())
                    dve.scalar_tensor_tensor(lraw[:, :], pLow[:, HR:LOWN], rs2[:, :], br_sb[:, :],
                                             ALU.mult, ALU.add).then_inc(v_lraw, 1)
                if c.exists():
                    wait(dve, a_ln, c.count())
                    dve.scalar_tensor_tensor(shift[c.r2][:, :], top8[:, :, 0], -1.0, lnsum[:, :],
                                             ALU.mult, ALU.subtract).then_inc(v_shift, 1)
                if ffn_here:
                    wait(dve, v_lraw, e.seqs())
                    dve.reduce_max(lmax[:, :], lraw[:, :], AX.X).then_inc(v_lmax, 1)
                    wait(dve, v_lmax, e.seqs())
                    dve.tensor_scalar(lg[:, :], lraw[:, :], lmax[:, :], None, ALU.subtract).then_inc(v_lg, 1)
                if s.half == 0 and nxt.exists():
                    statistics(nxt)
                if h.exists():
                    mine = x2[h.seq_r2][:, cols[h.half]]
                    if h.half == 0:
                        wait(dve, g_out, h.seqs(2, -4))
                    wait(dve, t_O, h.count())
                    dve.tensor_tensor(mine, pO[:, :], X[:, bass.ds(h.col(h.half), GW)], ALU.add).then_inc(v_x2, 1)
                    wait(dve, v_x2, h.count())
                    dve.bn_stats(st2[:, h.half, :], mine).then_inc(v_st, 1)
                if ffn_here:
                    wait(dve, a_le, e.seqs())
                    dve.reciprocal(lrec[:, :], lsum[:, :]).then_inc(v_lrec, 1)
                    wait(dve, v_lrec, e.seqs())
                    dve.tensor_scalar(sc[:, :], le[:, :], lrec[:, :], GAIN, ALU.mult, ALU.mult).then_inc(v_sc, 1)
                    wait(dve, v_sc, e.seqs())
                    dve.scalar_tensor_tensor(z[:, :, :], pLow[:, 0:HR].rearrange("p (h r) -> p h r", h=HEADS), rs2[:, :],
                                             sc[:, :].rearrange("p (h a) -> p h a", a=1).broadcast_to([128, HEADS, RANK]),
                                             ALU.mult, ALU.mult).then_inc(v_z, 1)
                if s.exists() and not early:
                    products(s)
                if ffn_here:
                    wait(dve, a_zT, e.seqs())
                    dve.tensor_tensor(zThl[1][:, :], pZ, zThl[0][:, :].bitcast(FP32), ALU.subtract).then_inc(v_zTlo, 1)
                if h.half == 1 and h.exists():
                    wait_apart(dve, v_st, h.count())
                    dve.bn_aggr(mv2[:, :], st2[:, :, :]).then_inc(v_mv2, 1)

            dve.memset(ninth[:, :, :], NEG).then_inc(v_init, 1)
            dve.wait_ge(v_init, 1)
            slots(dve, slot, {-1: lambda: statistics(At(0, 0)), 0: first_slot, 3: split_B})


_INS = ["x", "ctx_4096", "L0_ffn_A", "L0_ffn_B", "L0_ffn_Wr", "L0_ffn_br"]


def kernel(**inputs):
    import concourse.bacc as bacc
    from concourse.bass_utils import run_bass_kernel_spmd

    nc = bacc.Bacc("TRN2", target_bir_lowering=False, num_devices=1)
    arrays = {f"in_{n}": np.ascontiguousarray(inputs[n]) for n in _INS}
    arrays["in_mats"] = dft_matrices()
    args = [nc.dram_tensor(n, a.shape, mybir.dt.from_np(a.dtype), kind="ExternalInput").ap()
            for n, a in arrays.items()]
    out = nc.dram_tensor("out_0", (NSEQ, L, D), FP32, kind="ExternalOutput").ap()
    build(nc, *args, out)
    r = run_bass_kernel_spmd(nc, [arrays], core_ids=[0])
    return r.results[0]["out_0"]
```

```python
from contextlib import ExitStack

import numpy as np
import concourse.bass as bass
from concourse import mybir
from concourse.alu_op_type import AluOpType as ALU

FP32 = mybir.dt.float32
FP32R = mybir.dt.float32r
ACT = mybir.ActivationFunctionType
AX = mybir.AxisListType

NSEQ, L, D = 16, 128, 1024
GW = 512
NT = GW // 128
NG = NSEQ * D // GW
HEADS, RANK = 8, 16
HR = HEADS * RANK
LOWN = HR + HEADS
DC = D // 128
GAIN = float(HEADS) * 32.0 / RANK
TOPK = int(2 * np.log(L))
EPS = 1e-5
NEG = -3.0e38
SLOTS = 4
FIRST = 7
LOOPS = 5
WARM_UP = 2
DIRECT = 3
BY_POOL = 2 * (NSEQ - DIRECT)
SETS = ["F", "G", "Gv", "D1", "D2", "D3", "D4", "C1", "C2", "I"]
PRODUCTS = ("D1", "D2", "D3", "D4")
NSPLIT = 2
UNSPLIT = 2


def dft_matrices():
    n = np.arange(L)
    even = np.outer(np.arange(1, 64), n) * (2 * np.pi / L)
    odd = np.outer(2 * np.arange(64) + 1, n) * (np.pi / L)
    alt = (-1.0) ** n
    F = np.concatenate([np.ones((1, L)), np.cos(even), alt[None], -np.sin(even)])
    G = np.concatenate([np.cos(odd), -np.sin(odd)])
    Gv = G.copy()
    Gv[:, L - 1] -= G.sum(1)
    C1 = np.concatenate([np.ones((1, L)), 2 * np.cos(even), alt[None], 2 * np.cos(even)]) / L
    zero = np.zeros((1, L))
    C2 = np.concatenate([zero, 2 * np.sin(even), zero, -2 * np.sin(even)]) / L
    D1 = C1 / 2
    D2 = -C2 / 2
    D2[0] = 0.5
    D3 = np.concatenate([np.cos(odd), np.cos(odd)]) / L
    D4 = np.concatenate([-np.sin(odd), np.sin(odd)]) / L
    mats = dict(F=F.T, G=G.T, Gv=Gv.T, C1=C1, C2=C2, D1=D1, D2=D2, D3=D3, D4=D4, I=np.eye(L))
    return np.ascontiguousarray(np.concatenate([mats[k] for k in SETS], 1).astype(np.float32))


def build(nc, x, ctx, A, B, Wr, br, mats, out):
    es = ExitStack()
    with es:
        def sb(name, shape, dtype=FP32):
            return es.enter_context(nc.sbuf_tensor(name, shape, dtype))

        def ps(name, shape):
            return es.enter_context(nc.psum_tensor(name, shape, FP32))

        def sem(name):
            return es.enter_context(nc.semaphore(name))

        M_sb = sb("M_sb", [128, len(SETS) * L])
        M = {k: M_sb[:, i * L:(i + 1) * L] for i, k in enumerate(SETS)}
        SPLIT = SETS[:3 + NSPLIT]
        Mhl = [sb(f"M{p}", [128, len(SPLIT) * L], FP32R) for p in ("hi", "lo")]
        MS = {k: [m[:, i * L:(i + 1) * L] for m in Mhl] for i, k in enumerate(SPLIT)}
        X = sb("X", [128, NSEQ * D])
        CTX = [sb(f"CTX{i}", [128, D]) for i in range(2)]
        Chl = [[sb(f"C{p}{i}", [128, GW], FP32R) for p in ("hi", "lo")] for i in range(2)]
        q = sb("q", [128, GW])
        qhl = [sb(f"q{p}", [128, GW], FP32R) for p in ("hi", "lo")]
        K = [sb(f"K{i}", [128, GW]) for i in range(SLOTS)]
        Ks = [sb(f"Ks{i}", [128, GW]) for i in range(SLOTS)]
        V = [sb(f"V{i}", [128, GW]) for i in range(SLOTS)]
        Vs = [sb(f"Vs{i}", [128, GW]) for i in range(SLOTS)]
        QK = sb("QK", [128, 2, GW])
        top8 = sb("top8", [128, NT, 8])
        ninth = sb("ninth", [128, NT, 8])
        left1 = sb("left1", [128, NT, L])
        left2 = [sb(f"left2{i}", [128, NT, L]) for i in range(2)]
        E = [sb(f"E{i}", [128, NT, L]) for i in range(2)]
        dtop = sb("dtop", [128, NT, TOPK])
        etop = sb("etop", [128, NT, TOPK])
        stop = sb("stop", [128, NT])
        lnsum = sb("lnsum", [128, NT])
        shift = [sb(f"shift{i}", [128, NT]) for i in range(2)]
        WT = sb("WT", [128, GW])
        WThl = [sb(f"WT{p}", [128, GW], FP32R) for p in ("hi", "lo")]
        PW = sb("PW", [128, 4, GW])
        PWhl = [[sb(f"PW{p}{i}", [128, GW], FP32R) for p in ("hi", "lo")] for i in range(NSPLIT)]
        x2 = [sb(f"x2{i}", [128, D]) for i in range(2)]
        xT = [sb(f"xT{i}", [128, GW]) for i in range(2)]
        ABT = sb("ABT", [128, DC, LOWN])
        BT = sb("BT", [128, D])
        BThl = [sb(f"BT{p}", [128, D], FP32R) for p in ("hi", "lo")]
        pw = PW[:, :, :].rearrange("p (a b) c -> p a (b c)", a=2)
        A_sb, W_sb = pw[:, 0, :], pw[0:HEADS, 1, :]
        B_sb = x2[0][:, :].rearrange("p (h c r) -> p h c r", h=HEADS, r=RANK)
        B_by = x2[1][:, :].rearrange("p (c h r) -> p c h r", h=HEADS, r=RANK)
        br_sb = sb("br_sb", [128, HEADS])
        mean_of = sb("mean_of", [128, 128])
        consts = sb("consts", [128, 3])
        st1 = sb("st1", [128, 2, 6])
        mv1 = [sb(f"mv1{i}", [128, 2]) for i in range(2)]
        nm1 = sb("nm1", [128, 2])
        rs1 = [sb(f"rs1{i}", [128, 2]) for i in range(2)]
        st2 = sb("st2", [128, 2, 6])
        mv2 = sb("mv2", [128, 2])
        ve2 = sb("ve2", [128, 1])
        rs2 = sb("rs2", [128, 1])
        lraw = sb("lraw", [128, HEADS])
        lg = sb("lg", [128, HEADS])
        lmax = sb("lmax", [128, 1])
        le = sb("le", [128, HEADS])
        lsum = sb("lsum", [128, 1])
        lrec = sb("lrec", [128, 1])
        sc = sb("sc", [128, HEADS])
        z = sb("z", [128, HEADS, RANK])
        ffn = sb("ffn", [128, D])
        zThl = [sb(f"zT{p}", [128, 128], FP32R) for p in ("hi", "lo")]

        pKV = ps("pKV", [128, GW])
        pQ = ps("pQ", [128, GW])
        pC = ps("pC", [128, NT, L])
        pT = ps("pT", [128, GW])
        pWc = ps("pWc", [128, GW])
        pWn = ps("pWn", [128, GW])
        pO = ps("pO", [128, GW])
        pL = ps("pL", [128, GW])
        setup_banks = (pT, pO, pWc, pWn)
        pLow, pZ = pL[:, 0:LOWN], pL[:, 256:384]

        d_mat, d_mat2, d_AW, d_B, d_first = (sem("d_" + n) for n in "mat mat2 AW B first".split())
        d_x = [sem(f"d_x{i}") for i in range(2)]
        d_ctx = [sem(f"d_ctx{i}") for i in range(2)]
        d_ks = [sem(f"d_ks{i}") for i in range(SLOTS)]
        d_vs = [sem(f"d_vs{i}") for i in range(SLOTS)]
        d_out = sem("d_out")
        t_setup, t_mean, t_K, t_Q, t_V, t_C, t_WT, t_Wc, t_Wn, t_O, t_XT, t_low, t_zT, t_F = (
            sem("t_" + n) for n in "setup mean K Q V C WT Wc Wn O XT low zT F".split())
        a_setup, a_BThi, a_Chi, a_q, a_K, a_V, a_etop, a_ln, a_E, a_left = (
            sem("a_" + n) for n in "setup BThi Chi q K V etop ln E left".split())
        a_WT, a_WThi, a_PWhi, a_XT, a_le, a_zT, a_F = (
            sem("a_" + n) for n in "WT WThi PWhi XT le zT F".split())
        v_init, v_apart, v_Mhi, v_M, v_B, v_ABT = (
            sem("v_" + n) for n in "init apart Mhi M B ABT".split())
        v_stat, v_stats, v_QK, v_top, v_left1, v_nine, v_left2, v_dtop, v_stop, v_shift = (
            sem("v_" + n) for n in "stat stats QK top left1 nine left2 dtop stop shift".split())
        v_PW, v_x2, v_st, v_mv2, v_lraw, v_lmax, v_lg, v_lrec, v_sc, v_z, v_zTlo, v_out = (
            sem("v_" + n) for n in "PW x2 st mv2 lraw lmax lg lrec sc z zTlo out".split())
        g_setup, g_BTlo, g_rsa, g_rs1, g_qlo, g_W, g_WTlo, g_PWlo, g_rsb, g_rs2, g_out = (
            sem("g_" + n) for n in "setup BTlo rsa rs1 qlo W WTlo PWlo rsb rs2 out".split())
        c_Clo = sem("c_Clo")

        block = es.enter_context(nc.Block())

        class At:

            def __init__(self, j, off):
                self.j, self.off = j, off
                self.half = off % 2
                self.r2, self.r4 = off % 2, off % 4
                self.seq_r2 = off // 2 % 2

            def __sub__(self, lag):
                return At(self.j, self.off - lag)

            def __add__(self, lead):
                return At(self.j, self.off + lead)

            def exists(self):
                return not isinstance(self.j, int) or 0 <= SLOTS * self.j + self.off < NG

            def is_first(self):
                return isinstance(self.j, int) and SLOTS * self.j + self.off == 0

            def count(self, each=1, more=0):
                return self.j * (SLOTS * each) + ((self.off + 1) * each + more)

            def seqs(self, each=1, more=0):
                return self.j * (SLOTS // 2 * each) + ((self.off // 2 + 1) * each + more)

            def turns(self, each):
                return self.j * each + (self.off // SLOTS + 1) * each

            def seq(self):
                return self.j * (SLOTS // 2) + self.off // 2

            def col(self, half=0):
                return self.j * (SLOTS // 2 * D) + (self.off // 2 * D + half * GW)

        def wait(eng, semaphore, value):
            if not isinstance(value, int) or value > 0:
                eng.wait_ge(semaphore, value)

        def wait_apart(eng, semaphore, value):
            wait(eng, semaphore, value)
            if not isinstance(value, int):
                eng.sem_inc(v_apart, 1)

        def split_product(bank, left, right, start=True, stop=True):
            (lh, ll), (rh, rl) = left, right
            nc.tensor.matmul(bank, lh, rh, start=start, stop=False)
            nc.tensor.matmul(bank, lh, rl, start=False, stop=False)
            return nc.tensor.matmul(bank, ll, rh, start=False, stop=stop)

        def slots(eng, one_slot, setup={}):
            for s in range(-1, FIRST):
                if s in setup:
                    setup[s]()
                one_slot(At(0, s))
            with eng.Fori(0, LOOPS) as j:
                for k in range(SLOTS):
                    one_slot(At(j, FIRST + k))
            for s in range(FIRST, NG + 5 - SLOTS * LOOPS):
                one_slot(At(LOOPS, s))

        def splits(h):
            in_loop = not isinstance(h.j, int)
            return NSPLIT if in_loop or UNSPLIT <= SLOTS * h.j + h.off < NG - 3 else 0

        cols = [slice(h * GW, (h + 1) * GW) for h in range(2)]
        tiles = [slice(t * 128, (t + 1) * 128) for t in range(NT)]

        @block.sync
        def _(sp):
            sp.dma_start(X[:, 0:D], x[0]).then_inc(d_x[0], 16)
            sp.dma_start(M_sb[:, 0:len(SPLIT) * L], mats[:, 0:len(SPLIT) * L]).then_inc(d_mat, 16)
            sp.dma_start(CTX[0][:, cols[0]], ctx[0][:, cols[0]]).then_inc(d_first, 16)
            sp.dma_start(M_sb[:, len(SPLIT) * L:], mats[:, len(SPLIT) * L:]).then_inc(d_mat2, 16)
            sp.dma_start(CTX[0][:, cols[1]], ctx[0][:, cols[1]]).then_inc(d_ctx[0], 16)
            sp.dma_start(A_sb, A.rearrange("h r d -> (h r) d")).then_inc(d_AW, 16)
            sp.dma_start(W_sb, Wr).then_inc(d_AW, 16)

            def less_urgent():
                sp.dma_start(X[:, D:2 * D], x[1]).then_inc(d_x[1], 16)
                sp.dma_start(br_sb[:, :], br.partition_broadcast(128)).then_inc(d_B, 16)
                sp.dma_start(B_sb.rearrange("p h c r -> p h (c r)"),
                             B.rearrange("h (p c) r -> p h (c r)", p=128)).then_inc(d_B, 16)
                sp.dma_start(CTX[1][:, :], ctx[1]).then_inc(d_ctx[1], 16)

            def slot(s):
                if s.exists():
                    r = s.r4
                    wait(sp, a_K, s.count())
                    sp.dma_start(Ks[r][1:64, :], K[r][65:128, :]).then_inc(d_ks[r], 16)
                    sp.dma_start(Ks[r][64:128, :], K[r][0:64, :]).then_inc(d_ks[r], 16)
                    sp.dma_start(Ks[r][0:1, :], CTX[s.seq_r2][127:128, cols[s.half]]).then_inc(d_ks[r], 16)
                    if s.is_first():
                        less_urgent()
                    wait(sp, a_V, s.count())
                    sp.dma_start(Vs[r][0:64, :], V[r][64:128, :]).then_inc(d_vs[r], 16)
                    sp.dma_start(Vs[r][64:128, :], V[r][0:64, :]).then_inc(d_vs[r], 16)
                nxt = s + 4
                if s.half == 1 and s.exists() and nxt.exists():
                    r = s.seq_r2
                    for g in (s - 1, s):
                        wait(sp, d_ks[g.r4], g.turns(48))
                    sp.dma_start(CTX[r][:, :],
                                 ctx[bass.ds(nxt.seq(), 1)].rearrange("a p d -> (a p) d")).then_inc(d_ctx[r], 16)
                if s.is_first():
                    sp.wait_ge(d_x[0], 16)
                    sp.dma_start(X[:, 2 * D:3 * D], x[2]).then_inc(d_x[0], 16)
                nxt = s + 6
                if s.half == 1 and s.exists() and nxt.exists():
                    r = nxt.seq_r2
                    wait(sp, d_x[r], (s + 2).turns(16))
                    sp.dma_start(X[:, bass.ds(nxt.col(), D)],
                                 x[bass.ds(nxt.seq(), 1)].rearrange("a p d -> (a p) d")).then_inc(d_x[r], 16)
                f = s - 5
                if f.half == 1 and f.exists() and s.exists():
                    wait(sp, g_out, f.seqs(2))
                    sp.dma_start(out[bass.ds(f.seq(), 1)].rearrange("a p d -> (a p) d"),
                                 X[:, bass.ds(f.col(), D)]).then_inc(d_out, 16)
                elif f.half == 1 and f.exists():
                    for b in range(2):
                        wait(sp, v_out, f.seqs(2, b - 1 - BY_POOL))
                        sp.dma_start(out[f.seq(), :, cols[b]], X[:, bass.ds(f.col(b), GW)]).then_inc(d_out, 16)

            slots(sp, slot)
            sp.wait_ge(d_out, 16 * (NSEQ + DIRECT))

        @block.tensor
        def _(pe):
            mm = nc.tensor.matmul

            def weights_A():
                pe.wait_ge(d_mat2, 16)
                pe.wait_ge(d_AW, 32)
                for u in range(DC // 2):
                    for c in (2 * u, 2 * u + 1):
                        at, to = slice(c * 128, (c + 1) * 128), c % 2 * LOWN
                        nc.tensor.transpose(setup_banks[u][:, to:to + HR], A_sb[:, at], M["I"])
                        last = nc.tensor.transpose(setup_banks[u][:, to + HR:to + LOWN], W_sb[:, at],
                                                   M["I"][0:HEADS, 0:HEADS])
                    last.then_inc(t_setup, 1)

            def weights_B():
                pe.wait_ge(a_setup, DC // 2)
                pe.wait_ge(g_setup, 4)
                for c in range(DC):
                    last = mm(pO[:, 0:LOWN], mean_of[:, :], ABT[:, c, :], start=(c == 0), stop=(c == DC - 1))
                last.then_inc(t_mean, 1)
                pe.wait_ge(v_B, 1)
                for u in range(2):
                    for c in range(4):
                        last = nc.tensor.transpose(setup_banks[2 + u][:, tiles[c]],
                                                   B_by[:, 4 * u + c, :, :].rearrange("p h r -> p (h r)"), M["I"])
                    last.then_inc(t_setup, 1)

            def busy(count):
                for _ in range(count):
                    mm(pWn[:, :], X[:, 0:128], X[:, 0:GW], start=True, stop=True)

            def slot(s):
                c, g, h, e, f = s - 1, s - 2, s - 3, s - 4, s - 5
                if e.exists():
                    wait(pe, v_x2, e.count())
                    for t in range(NT):
                        at = e.half * GW + t * 128
                        last = nc.tensor.transpose(pO[:, tiles[t]], x2[e.seq_r2][:, at:at + 128], M["I"])
                    last.then_inc(t_XT, 1)
                if s.exists():
                    ctx_halves = [m[:, :] for m in Chl[s.r2]]
                    wait(pe, c_Clo, s.count())
                    wait(pe, a_V, s.count(1, -1))
                    split_product(pKV[:, :], MS["F"], ctx_halves).then_inc(t_K, 1)
                if f.half == 1 and f.exists():
                    if not h.exists():
                        wait(pe, v_out, f.seqs(2, -2 - BY_POOL))
                        busy(WARM_UP)
                    wait(pe, v_z, f.seqs())
                    nc.tensor.transpose(pZ, z[:, :, :].rearrange("p h r -> p (h r)"), M["I"]).then_inc(t_zT, 1)
                if c.exists():
                    wait(pe, v_QK, c.count(2))
                    wait(pe, a_E, c.count(1, -1))
                    for t in range(NT):
                        mm(pC[:, t, :], QK[:, 0, tiles[t]], M["C1"], start=True, stop=False)
                        last = mm(pC[:, t, :], QK[:, 1, tiles[t]], M["C2"], start=False, stop=True)
                    last.then_inc(t_C, 1)
                if g.exists():
                    wait(pe, g_W, g.count(2))
                    for t in range(NT):
                        last = nc.tensor.transpose(pT[:, tiles[t]], E[g.r2][:, t, :], M["I"])
                    last.then_inc(t_WT, 1)
                if e.half == 1 and e.exists():
                    wait(pe, a_XT, e.count())
                    for t in range(NT):
                        chunk = e.half * NT + t
                        last = mm(pLow, xT[e.r2][:, tiles[t]], ABT[:, chunk, :],
                                  start=(chunk == 0), stop=(chunk == DC - 1))
                    last.then_inc(t_low, 1)
                if h.exists():
                    if e.exists():
                        wait(pe, a_XT, e.count())
                    for p in range(splits(h), 4):
                        wait(pe, v_PW, h.count(4, p - 3))
                        last = mm(pO[:, :], M[PRODUCTS[p]], PW[:, p, :],
                                  start=(p == splits(h)), stop=(splits(h) == 0 and p == 3))
                    if not splits(h):
                        last.then_inc(t_O, 1)
                if e.half == 0 and e.exists():
                    wait(pe, a_XT, e.count())
                    wait(pe, v_zTlo, e.seqs(1, -1))
                    for t in range(NT):
                        chunk = e.half * NT + t
                        last = mm(pLow, xT[e.r2][:, tiles[t]], ABT[:, chunk, :],
                                  start=(chunk == 0), stop=(chunk == DC - 1))
                if h.exists() and splits(h):
                    for p in range(splits(h)):
                        wait(pe, g_PWlo, h.count(NSPLIT, p + 1 - NSPLIT * (1 + UNSPLIT)))
                        last = split_product(pO[:, :], MS[PRODUCTS[p]], [m[:, :] for m in PWhl[p]],
                                             start=False, stop=(p == splits(h) - 1))
                    last.then_inc(t_O, 1)
                if f.half == 1 and f.exists():
                    if not h.exists():
                        wait(pe, v_out, f.seqs(2, -2 - BY_POOL))
                    wait(pe, v_zTlo, f.seqs())
                    if h.exists():
                        wait(pe, v_PW, h.count(4))
                    for b, bank in enumerate((pWc, pWn)):
                        split_product(bank[:, :], [m[:, :] for m in zThl], [m[:, cols[b]] for m in BThl])\
                            .then_inc(t_F, 1)
                if s.exists():
                    wait(pe, g_qlo, s.count())
                    wait(pe, v_QK, s.count(2, -2))
                    split_product(pQ[:, :], MS["F"], [m[:, :] for m in qhl]).then_inc(t_Q, 1)
                    wait(pe, a_K, s.count())
                    split_product(pKV[:, :], MS["Gv"], ctx_halves).then_inc(t_V, 1)
                if g.exists():
                    w_halves = [m[:, :] for m in WThl]
                    wait(pe, g_WTlo, g.count())
                    if not h.exists():
                        wait(pe, a_setup, DC // 2 + 2)
                    if f.half == 1 and f.exists():
                        left_banks = (a_F, 0) if s.exists() else (v_out, BY_POOL)
                        wait(pe, left_banks[0], f.seqs(2, -1 - left_banks[1]))
                    split_product(pWc[:, :], MS["F"], w_halves).then_inc(t_Wc, 1)
                    if f.half == 1 and f.exists():
                        wait(pe, left_banks[0], f.seqs(2, -left_banks[1]))
                    split_product(pWn[:, :], MS["G"], w_halves).then_inc(t_Wn, 1)

            pe.wait_ge(d_x[0], 16)
            busy(WARM_UP)
            pe.wait_ge(v_M, 1)
            slots(pe, slot, {1: weights_A, 2: weights_B,
                             4: lambda: pe.wait_ge(v_ABT, 1),
                             6: lambda: pe.wait_ge(g_BTlo, 2)})

        @block.scalar
        def _(act):
            act.preload_act_table_set("natural_log_exp_and_others")

            def weights_A():
                for u in range(DC // 2):
                    act.wait_ge(t_setup, u + 1)
                    act.copy(ABT[:, 2 * u:2 * u + 2, :],
                             setup_banks[u][:, 0:2 * LOWN].rearrange("p (c n) -> p c n", c=2)).then_inc(a_setup, 1)

            def weights_B():
                for u in range(2):
                    act.wait_ge(t_setup, DC // 2 + u + 1)
                    act.copy(BT[:, :].rearrange("k (p c) -> k c p", c=DC)[:, 4 * u:4 * u + 4, :],
                             setup_banks[2 + u][:, :].rearrange("k (c p) -> k c p", c=4)).then_inc(a_setup, 1)

            def B_high():
                act.wait_ge(a_setup, DC // 2 + 2)
                act.copy(BThl[0][:, :], BT[:, :]).then_inc(a_BThi, 1)

            def copy_V(s):
                if s.exists():
                    wait(act, t_V, s.count())
                    act.copy(V[s.r4][:, :], pKV[:, :]).then_inc(a_V, 1)

            def layernorm(n):
                if n.exists():
                    wait(act, g_rs1, n.seqs())
                    for to in (q, qhl[0]):
                        act.activation(to[:, :], X[:, bass.ds(n.col(n.half), GW)], ACT.Identity,
                                       bias=rs1[n.seq_r2][:, 1:2], scale=rs1[n.seq_r2][:, 0:1]).then_inc(a_q, 1)

            def slot(s):
                c, g, h, e, f, n = s - 1, s - 2, s - 3, s - 4, s - 5, s + 1
                if e.exists():
                    wait(act, t_XT, e.count())
                    act.copy(xT[e.r2][:, :], pO[:, :]).then_inc(a_XT, 1)
                if s.exists():
                    wait(act, t_K, s.count())
                    act.copy(K[s.r4][:, :], pKV[:, :]).then_inc(a_K, 1)
                if f.half == 1 and f.exists():
                    wait(act, t_zT, f.seqs())
                    act.copy(zThl[0][:, :], pZ).then_inc(a_zT, 1)
                if h.exists():
                    for p in range(splits(h)):
                        wait(act, v_PW, h.count(4, p - 3))
                        act.copy(PWhl[p][0][:, :], PW[:, p, :]).then_inc(a_PWhi, 1)
                if n.exists():
                    if not s.exists():
                        act.wait_ge(d_first, 16)
                    elif n.half == 0 or not c.exists():
                        wait(act, d_ctx[n.seq_r2], n.turns(16))
                    act.copy(Chl[n.r2][0][:, :], CTX[n.seq_r2][:, cols[n.half]]).then_inc(a_Chi, 1)
                if g.exists():
                    wait(act, t_WT, g.count())
                    act.copy(WThl[0][:, :], pT[:, :]).then_inc(a_WThi, 1)
                    act.copy(WT[:, :], pT[:, :]).then_inc(a_WT, 1)
                V_early = c.exists() and not h.exists()
                q_early = c.exists() and not g.exists()
                if V_early:
                    copy_V(s)
                if q_early:
                    layernorm(n)
                if c.exists():
                    wait(act, v_dtop, c.count())
                    act.activation(etop[:, :, :], dtop[:, :, :], ACT.Exp).then_inc(a_etop, 1)
                if c.exists():
                    wait(act, v_stop, c.count())
                    act.activation(lnsum[:, :], stop[:, :], ACT.Ln).then_inc(a_ln, 1)
                if c.exists():
                    wait(act, v_shift, c.count())
                    for k in range(NT):
                        last = act.activation(E[c.r2][:, k, :], pC[:, k, :], ACT.Exp, bias=shift[c.r2][:, k:k + 1])
                    last.then_inc(a_E, 1)
                if e.half == 1 and e.exists():
                    wait(act, v_lg, e.seqs())
                    act.activation(le[:, :], lg[:, :], ACT.Exp, accum_out=lsum[:, :]).then_inc(a_le, 1)
                V_after = 0 if s.half == 1 else 1
                for u in range(2):
                    if f.half == 1 and f.exists() and s.exists():
                        wait(act, g_out, f.seqs(2, u - 3))
                        wait(act, t_F, f.seqs(2, u - 1))
                        act.copy(ffn[:, cols[u]], (pWc, pWn)[u][:, :]).then_inc(a_F, 1)
                    if c.exists():
                        for k in (2 * u, 2 * u + 1):
                            last = act.activation(left2[c.r2][:, k, :], left2[c.r2][:, k, :], ACT.Exp,
                                                  bias=shift[c.r2][:, k:k + 1])
                        last.then_inc(a_left, 1)
                    if u == V_after and not V_early:
                        copy_V(s)
                if not q_early:
                    layernorm(n)

            slots(act, slot, {1: weights_A, 2: weights_B, 4: B_high})

        @block.gpsimd
        def _(pool):
            def rstd(n):
                mv, rs = mv1[n.seq_r2], rs1[n.seq_r2]
                wait(pool, v_stats, n.seqs())
                pool.tensor_tensor(nm1[:, 0:1], mv[:, 0:1], consts[:, 1:2], ALU.mult).then_inc(g_rsa, 1)
                pool.tensor_tensor(nm1[:, 1:2], mv[:, 1:2], consts[:, 2:3], ALU.add).then_inc(g_rsa, 1)
                wait(pool, g_rsa, n.seqs(3, -1))
                pool.tensor_tensor(rs[:, 0:1], nm1[:, 1:2], consts[:, 0:1], ALU.pow).then_inc(g_rsa, 1)
                wait(pool, g_rsa, n.seqs(3))
                pool.tensor_tensor(rs[:, 1:2], nm1[:, 0:1], rs[:, 0:1], ALU.mult).then_inc(g_rs1, 1)

            def result(f, s, b):
                if f.half == 1 and f.exists() and s.exists():
                    wait(pool, a_F, f.seqs(2, b - 1))
                    pool.tensor_tensor(X[:, bass.ds(f.col(b), GW)], ffn[:, cols[b]],
                                       x2[f.seq_r2][:, cols[b]], ALU.add).then_inc(g_out, 1)

            def slot(s):
                c, g, h, f, n = s - 1, s - 2, s - 3, s - 5, s + 1
                if h.exists():
                    for p in range(splits(h)):
                        hi, lo = PWhl[p]
                        wait(pool, a_PWhi, h.count(NSPLIT, p + 1 - NSPLIT * (1 + UNSPLIT)))
                        pool.tensor_tensor(lo[:, :], PW[:, p, :], hi[:, :].bitcast(FP32),
                                           ALU.subtract).then_inc(g_PWlo, 1)
                if s.exists():
                    hi, lo = qhl
                    wait(pool, a_q, s.count(2))
                    pool.tensor_tensor(lo[:, :], q[:, :], hi[:, :].bitcast(FP32),
                                       ALU.subtract).then_inc(g_qlo, 1)
                if g.exists():
                    hi, lo = WThl
                    wait(pool, a_WT, g.count())
                    pool.tensor_tensor(lo[:, :], WT[:, :], hi[:, :].bitcast(FP32),
                                       ALU.subtract).then_inc(g_WTlo, 1)
                if n.half == 0 and n.exists() and not h.exists():
                    rstd(n)
                if s.exists() and n.exists():
                    hi, lo = Chl[n.r2]
                    wait(pool, a_Chi, n.count())
                    pool.tensor_tensor(lo[:, :], CTX[n.seq_r2][:, cols[n.half]], hi[:, :].bitcast(FP32),
                                       ALU.subtract).then_inc(c_Clo, 1)
                if n.half == 0 and n.exists() and h.exists():
                    rstd(n)
                result(f, s, 0)
                if c.exists():
                    for u in range(2):
                        at = slice(2 * u, 2 * u + 2)
                        wait(pool, a_left, c.count(2, u - 1))
                        pool.tensor_tensor(E[c.r2][:, at, :], E[c.r2][:, at, :], left2[c.r2][:, at, :],
                                           ALU.subtract).then_inc(g_W, 1)
                if h.half == 1 and h.exists():
                    wait(pool, v_mv2, h.seqs())
                    pool.tensor_tensor(ve2[:, :], mv2[:, 1:2], consts[:, 2:3], ALU.add).then_inc(g_rsb, 1)
                    wait(pool, g_rsb, h.seqs())
                    pool.tensor_tensor(rs2[:, :], ve2[:, :], consts[:, 0:1], ALU.pow).then_inc(g_rs2, 1)
                result(f, s, 1)

            for i, value in enumerate((-0.5, -1.0, EPS)):
                pool.memset(consts[:, i:i + 1], value).then_inc(g_setup, 1)
            pool.memset(mean_of[:, :], 1.0 / D).then_inc(g_setup, 1)
            pool.wait_ge(g_setup, 4)

            def B_low(b):
                pool.wait_ge(a_BThi, 1)
                pool.tensor_tensor(BThl[1][:, cols[b]], BT[:, cols[b]], BThl[0][:, cols[b]].bitcast(FP32),
                                   ALU.subtract).then_inc(g_BTlo, 1)

            slots(pool, slot, {4: lambda: B_low(0), 5: lambda: B_low(1)})

        @block.vector
        def _(dve):
            def first_slot():
                dve.wait_ge(d_mat, 16)
                to_split = slice(0, len(SPLIT) * L)
                dve.tensor_copy(Mhl[0][:, :], M_sb[:, to_split]).then_inc(v_Mhi, 1)
                dve.wait_ge(v_Mhi, 1)
                dve.tensor_tensor(Mhl[1][:, :], M_sb[:, to_split], Mhl[0][:, :].bitcast(FP32),
                                  ALU.subtract).then_inc(v_M, 1)
                hi, lo = Chl[0]
                dve.wait_ge(a_Chi, 1)
                dve.tensor_tensor(lo[:, :], CTX[0][:, cols[0]], hi[:, :].bitcast(FP32),
                                  ALU.subtract).then_inc(c_Clo, 1)

            def weights():
                dve.wait_ge(d_B, 32)
                dve.tensor_copy(B_by.rearrange("p c h r -> p h c r"), B_sb).then_inc(v_B, 1)

            def centre():
                dve.wait_ge(t_mean, 1)
                mean = pO[:, 0:LOWN].rearrange("p (a n) -> p a n", a=1).broadcast_to([128, DC, LOWN])
                dve.tensor_tensor(ABT[:, :, :], ABT[:, :, :], mean, ALU.subtract).then_inc(v_ABT, 1)

            def statistics(n):
                wait(dve, d_x[n.seq_r2], n.turns(16))
                for b in range(2):
                    dve.bn_stats(st1[:, b, :], X[:, bass.ds(n.col(b), GW)]).then_inc(v_stat, 1)
                wait_apart(dve, v_stat, n.seqs(2))
                dve.bn_aggr(mv1[n.seq_r2][:, :], st1[:, :, :]).then_inc(v_stats, 1)

            def slot(s):
                c, h, e, f, nxt = s - 1, s - 3, s - 4, s - 5, s + 2
                ffn_here = e.half == 1 and e.exists()
                if h.exists():
                    r = h.r4
                    wait(dve, t_Wc, h.count())
                    dve.tensor_tensor(PW[:, 0, :], pWc[:, :], K[r][:, :], ALU.mult).then_inc(v_PW, 1)
                    dve.tensor_tensor(PW[:, 1, :], pWc[:, :], Ks[r][:, :], ALU.mult).then_inc(v_PW, 1)
                    wait(dve, t_Wn, h.count())
                    wait(dve, a_V, h.count())
                    dve.tensor_tensor(PW[:, 2, :], pWn[:, :], V[r][:, :], ALU.mult).then_inc(v_PW, 1)
                    wait(dve, d_vs[r], h.turns(32))
                    dve.tensor_tensor(PW[:, 3, :], pWn[:, :], Vs[r][:, :], ALU.mult).then_inc(v_PW, 1)
                if f.half == 1 and f.exists():
                    wait(dve, a_zT, f.seqs())
                    dve.tensor_tensor(zThl[1][:, :], pZ, zThl[0][:, :].bitcast(FP32),
                                      ALU.subtract).then_inc(v_zTlo, 1)
                if c.exists():
                    wait_apart(dve, t_C, c.count())
                    for t in range(NT):
                        dve.max(top8[:, t, :], pC[:, t, :]).then_inc(v_top, 1)
                    wait(dve, v_top, c.count(NT))
                    dve.tensor_tensor(dtop[:, :, 0:8], top8[:, :, :], top8[:, :, 0:1].broadcast_to([128, NT, 8]),
                                      ALU.subtract)
                    for t in range(NT):
                        dve.match_replace(left1[:, t, :], top8[:, t, :], pC[:, t, :], NEG).then_inc(v_left1, 1)
                    wait(dve, v_left1, c.count(NT))
                    dve.reduce_max(ninth[:, :, 0:1], left1[:, :, :], AX.X).then_inc(v_nine, 1)
                    wait(dve, v_nine, c.count())
                    dve.tensor_tensor(dtop[:, :, 8:9], ninth[:, :, 0:1], top8[:, :, 0:1],
                                      ALU.subtract).then_inc(v_dtop, 1)
                    for t in range(NT):
                        dve.match_replace(left2[c.r2][:, t, :], ninth[:, t, :], left1[:, t, :], NEG)\
                           .then_inc(v_left2, 1)
                    wait(dve, a_etop, c.count())
                    dve.reduce_sum(stop[:, :], etop[:, :, :], AX.X).then_inc(v_stop, 1)
                if ffn_here:
                    wait(dve, t_low, e.seqs())
                    wait(dve, g_rs2, e.seqs())
                    dve.scalar_tensor_tensor(lraw[:, :], pLow[:, HR:LOWN], rs2[:, :], br_sb[:, :],
                                             ALU.mult, ALU.add).then_inc(v_lraw, 1)
                if c.exists():
                    wait(dve, a_ln, c.count())
                    dve.scalar_tensor_tensor(shift[c.r2][:, :], top8[:, :, 0], -1.0, lnsum[:, :],
                                             ALU.mult, ALU.subtract).then_inc(v_shift, 1)
                if ffn_here:
                    wait(dve, v_lraw, e.seqs())
                    dve.reduce_max(lmax[:, :], lraw[:, :], AX.X).then_inc(v_lmax, 1)
                    wait(dve, v_lmax, e.seqs())
                    dve.tensor_scalar(lg[:, :], lraw[:, :], lmax[:, :], None, ALU.subtract).then_inc(v_lg, 1)
                if s.half == 0 and nxt.exists() and h.exists():
                    statistics(nxt)
                if h.exists():
                    mine = x2[h.seq_r2][:, cols[h.half]]
                    if h.half == 0 and s.exists():
                        wait(dve, g_out, h.seqs(2, -4))
                    wait(dve, t_O, h.count())
                    dve.tensor_tensor(mine, pO[:, :], X[:, bass.ds(h.col(h.half), GW)], ALU.add).then_inc(v_x2, 1)
                if ffn_here:
                    wait(dve, a_le, e.seqs())
                    dve.reciprocal(lrec[:, :], lsum[:, :]).then_inc(v_lrec, 1)
                if h.exists():
                    wait(dve, v_x2, h.count())
                    dve.bn_stats(st2[:, h.half, :], mine).then_inc(v_st, 1)
                if ffn_here:
                    wait(dve, v_lrec, e.seqs())
                    dve.tensor_scalar(sc[:, :], le[:, :], lrec[:, :], GAIN, ALU.mult, ALU.mult).then_inc(v_sc, 1)
                if s.exists():
                    wait(dve, t_Q, s.count())
                    wait(dve, a_K, s.count())
                    dve.tensor_tensor(QK[:, 0, :], pQ[:, :], K[s.r4][:, :], ALU.mult).then_inc(v_QK, 1)
                if ffn_here:
                    wait(dve, v_sc, e.seqs())
                    dve.scalar_tensor_tensor(z[:, :, :], pLow[:, 0:HR].rearrange("p (h r) -> p h r", h=HEADS), rs2[:, :],
                                             sc[:, :].rearrange("p (h a) -> p h a", a=1).broadcast_to([128, HEADS, RANK]),
                                             ALU.mult, ALU.mult).then_inc(v_z, 1)
                if s.exists():
                    wait(dve, d_ks[s.r4], s.turns(48))
                    dve.tensor_tensor(QK[:, 1, :], pQ[:, :], Ks[s.r4][:, :], ALU.mult).then_inc(v_QK, 1)
                if s.half == 0 and nxt.exists() and not h.exists():
                    statistics(nxt)
                if h.half == 1 and h.exists():
                    wait_apart(dve, v_st, h.count())
                    dve.bn_aggr(mv2[:, :], st2[:, :, :]).then_inc(v_mv2, 1)
                if f.half == 1 and f.exists() and not s.exists():
                    for b in range(2):
                        wait(dve, t_F, f.seqs(2, b - 1))
                        dve.tensor_tensor(X[:, bass.ds(f.col(b), GW)], (pWc, pWn)[b][:, :],
                                          x2[f.seq_r2][:, cols[b]], ALU.add).then_inc(v_out, 1)

            dve.memset(ninth[:, :, :], NEG).then_inc(v_init, 1)
            dve.wait_ge(v_init, 1)
            slots(dve, slot, {-1: lambda: statistics(At(0, 0)), 0: first_slot, 1: weights, 2: centre})


_INS = ["x", "ctx_4096", "L0_ffn_A", "L0_ffn_B", "L0_ffn_Wr", "L0_ffn_br"]


def kernel(**inputs):
    import concourse.bacc as bacc
    from concourse.bass_utils import run_bass_kernel_spmd

    nc = bacc.Bacc("TRN2", target_bir_lowering=False, num_devices=1)
    arrays = {f"in_{n}": np.ascontiguousarray(inputs[n]) for n in _INS}
    arrays["in_mats"] = dft_matrices()
    args = [nc.dram_tensor(n, a.shape, mybir.dt.from_np(a.dtype), kind="ExternalInput").ap()
            for n, a in arrays.items()]
    out = nc.dram_tensor("out_0", (NSEQ, L, D), FP32, kind="ExternalOutput").ap()
    build(nc, *args, out)
    r = run_bass_kernel_spmd(nc, [arrays], core_ids=[0])
    return r.results[0]["out_0"]
```
